# Optimizing a Trainium2 kernel written in Bass

```python
import numpy as np
import jax
import jax.numpy as jnp

def _softmax(x, axis=-1):
    return jax.nn.softmax(x, axis=axis)

def _gelu(x):
    return jax.nn.gelu(x, approximate=True)

def _silu(x):
    return jax.nn.silu(x)

def _sigmoid(x):
    return jax.nn.sigmoid(x)

def _layernorm(x, axis=-1, eps=1e-05):
    m = jnp.mean(x, axis=axis, keepdims=True)
    v = jnp.var(x, axis=axis, keepdims=True)
    return (x - m) / jnp.sqrt(v + eps)

def _scatter_add(tgt, idx, src, axis=0):
    return tgt.at[idx].add(src)

def _segment_sum(src, seg, n):
    return jax.ops.segment_sum(src, seg, n)
kernel_name = 'mk_adaln_ffn_d1_seqx_r8_8eb6b4'

def setup_inputs(seed: int=0):
    np.random.seed(seed)
    _w = jnp.asarray

    def _rec_inputs():
        import jax
        import jax.numpy as jnp
        _rk = jax.random.key(seed)
        x = -0.0003929 + 0.9999 * jax.random.normal(jax.random.fold_in(_rk, 1), (2, 512, 128), jnp.float32)
        _lenS = 512 - jax.random.randint(jax.random.fold_in(_rk, 7), (2,), 0, max(1, 512 // 4) + 1, jnp.int32)
        _lenS2 = 512 - jax.random.randint(jax.random.fold_in(_rk, 8), (2,), 0, max(1, 512 // 4) + 1, jnp.int32)
        cond_1024 = 0.00513981 + 1.0024 * jax.random.normal(jax.random.fold_in(_rk, 11), (2, 128), jnp.float32)
        return (x, cond_1024)
    x, cond_1024 = _rec_inputs()

    def _L0_cond_setup():
        import jax, jax.numpy as jnp
        import numpy as np
        key = jax.random.key(seed)
        k1, k2, k3, k4 = jax.random.split(key, 4)
        B, L, D = (32, 64, 128)
        scale = 1.0 / np.sqrt(D)
        return {'x': jax.random.normal(k1, (B, L, D), dtype=jnp.float32), 'h0': jax.random.normal(k2, (B, D), dtype=jnp.float32), 'Wx': jax.random.normal(k3, (D, D), dtype=jnp.float32) * scale, 'Wh': jax.random.normal(k4, (D, D), dtype=jnp.float32) * scale}
    _L0_cond_all = _L0_cond_setup()
    _L0_cond_in = {k: v for k, v in _L0_cond_all.items() if k in ('Wx', 'Wh')}
    del _L0_cond_all

    def _L0_ffn_setup():
        import jax, jax.numpy as jnp
        import numpy as np
        DIM = 128
        NUM_EXPERTS = 8
        EXPERT_DIM = 384
        B, S = (1, 256)
        key = jax.random.key(seed)
        ks = jax.random.split(key, 7)
        sd = 0.02
        x = jax.random.normal(ks[0], (B, S, DIM), dtype=jnp.float32)
        Wr = jax.random.normal(ks[1], (DIM, NUM_EXPERTS), dtype=jnp.float32) * sd
        br = jnp.zeros((NUM_EXPERTS,), dtype=jnp.float32)
        W1 = jax.random.normal(ks[2], (NUM_EXPERTS, DIM, EXPERT_DIM), dtype=jnp.float32) * sd
        b1 = jnp.zeros((NUM_EXPERTS, EXPERT_DIM), dtype=jnp.float32)
        W2 = jax.random.normal(ks[3], (NUM_EXPERTS, EXPERT_DIM, DIM), dtype=jnp.float32) * sd
        b2 = jnp.zeros((NUM_EXPERTS, DIM), dtype=jnp.float32)
        return {'x': x, 'Wr': Wr, 'br': br, 'W1': W1, 'b1': b1, 'W2': W2, 'b2': b2}
    _L0_ffn_all = _L0_ffn_setup()
    _L0_ffn_in = {k: v for k, v in _L0_ffn_all.items() if k in ('Wr', 'br', 'W1', 'b1', 'W2', 'b2')}
    del _L0_ffn_all
    return {'x': x, 'cond_1024': cond_1024, 'L0_cond_Wx': _L0_cond_in['Wx'], 'L0_cond_Wh': _L0_cond_in['Wh'], 'L0_ffn_Wr': _L0_ffn_in['Wr'], 'L0_ffn_br': _L0_ffn_in['br'], 'L0_ffn_W1': _L0_ffn_in['W1'], 'L0_ffn_b1': _L0_ffn_in['b1'], 'L0_ffn_W2': _L0_ffn_in['W2'], 'L0_ffn_b2': _L0_ffn_in['b2']}

def reference(x, cond_1024, L0_cond_Wx, L0_cond_Wh, L0_ffn_Wr, L0_ffn_br, L0_ffn_W1, L0_ffn_b1, L0_ffn_W2, L0_ffn_b2):
    import jax
    import jax.numpy as jnp

    def _L0_cond_ref(x, h0, Wx, Wh):
        import jax, jax.numpy as jnp
        import numpy as np
        xp = jnp.einsum('bld,de->ble', x, Wx)

        def step(h, xt):
            h_new = jnp.tanh(xt + h @ Wh)
            return (h_new, h_new)
        _, hs = jax.lax.scan(step, h0, jnp.swapaxes(xp, 0, 1))
        return jnp.swapaxes(hs, 0, 1)

    def _L0_ffn_ref(x, Wr, br, W1, b1, W2, b2):
        import jax, jax.numpy as jnp
        import numpy as np
        DIM = 128
        NUM_EXPERTS = 8
        EXPERT_DIM = 384
        B, S = (1, 256)
        router_logits = x @ Wr + br
        expert_idx = jnp.argmax(router_logits, axis=-1)
        onehot = jax.nn.one_hot(expert_idx, NUM_EXPERTS, dtype=x.dtype)
        h = jax.nn.gelu(jnp.einsum('bsd,edh->bseh', x, W1) + b1, approximate=False)
        y = jnp.einsum('bseh,ehd->bsed', h, W2) + b2
        out = jnp.einsum('bsed,bse->bsd', y, onehot)
        return out
    x = x + _L0_ffn_ref(_L0_cond_ref(x, cond_1024, L0_cond_Wx, L0_cond_Wh), L0_ffn_Wr, L0_ffn_br, L0_ffn_W1, L0_ffn_b1, L0_ffn_W2, L0_ffn_b2)
    return x

_drawn_inputs = setup_inputs


def setup_inputs(seed=0):
    import zlib

    import numpy as np

    out = dict(_drawn_inputs(seed))
    spreads = {'L0_ffn_br': (0.0, 0.1), 'L0_ffn_b1': (0.0, 0.399), 'L0_ffn_b2': (0.0, 0.1)}
    factors = {'cond_1024': 8.0}
    for name, (base, spread) in spreads.items():
        noise = np.random.default_rng([zlib.crc32(name.encode()), seed]).standard_normal(out[name].shape)
        drawn = base * np.exp(spread * noise) if base else spread * noise
        out[name] = jnp.asarray(drawn.astype(out[name].dtype))
    for name, factor in factors.items():
        out[name] = (out[name] * factor).astype(out[name].dtype)
    return out
```

```python
import concourse.bass as bass
from concourse import mybir
from concourse.alu_op_type import AluOpType as ALU
from contextlib import ExitStack

F32 = mybir.dt.float32
BF16 = mybir.dt.bfloat16
ACT = mybir.ActivationFunctionType
AX = mybir.AxisListType

B, T, D = 2, 512, 128
E, H = 8, 384
KB = H // 128
C = 64
N = B * C
NCH = T // C


def build(nc, x, cond, Wx, Wh, Wr, br, W1, b1, W2, b2, out):
    ctx = ExitStack()
    with ctx:
        def sb(name, shape, dt=F32):
            return ctx.enter_context(nc.sbuf_tensor(name, shape, dt))

        def ps(name, shape, dt=F32):
            return ctx.enter_context(nc.psum_tensor(name, shape, dt))

        def sem(name):
            return ctx.enter_context(nc.semaphore(name))

        x_sb = sb("x_sb", [N, NCH, D])
        cond_sb = sb("cond_sb", [B, D])
        Wx_sb = sb("Wx_sb", [D, D])
        Wh_sb = sb("Wh_sb", [D, D])
        Wr_sb = sb("Wr_sb", [D, E])
        br_sb = sb("br_sb", [N, E])
        W1_sb = sb("W1_sb", [D, E, H])
        b1_sb = sb("b1_sb", [E, H])
        W2_sb = sb("W2_sb", [128, E, KB, D])
        b2_sb = sb("b2_sb", [E, D])
        ident = sb("ident", [128, 128])
        ident16 = sb("ident16", [128, 128], BF16)
        desc = sb("desc", [N, E])
        xT = sb("xT", [D, NCH, N])
        hT = sb("hT", [D, NCH + 1, B, C])
        logit = sb("logit", [N, E])
        top = sb("top", [N, 8])
        cand = sb("cand", [N, E])
        first = sb("first", [N, 1])
        onehot = sb("onehot", [N, E], BF16)
        onehotT = sb("onehotT", [E, N])
        hm = sb("hm", [D, E, N])
        g = sb("g", [128, KB, N])
        gm = sb("gm", [128, KB, E, N])
        y_sb = sb("y_sb", [N, NCH, D])
        pre = ps("pre", [128, 2, 512])
        mask = ps("mask", [128, E, N])
        z = ps("z", [128, 2, 512])
        y = ps("y", [128, 512])
        small = ps("small", [128, 4, 128])

        x0_loaded = sem("x0_loaded")
        x_loaded = sem("x_loaded")
        cond_loaded = sem("cond_loaded")
        wx_loaded = sem("wx_loaded")
        wh_loaded = sem("wh_loaded")
        wr_loaded = sem("wr_loaded")
        w1_loaded = sem("w1_loaded")
        w2_loaded = sem("w2_loaded")
        ident_zeroed = sem("ident_zeroed")
        ident_ready = sem("ident_ready")
        ident16_ready = sem("ident16_ready")
        desc_ready = sem("desc_ready")
        xT_made = sem("xT_made")
        xT_ready = sem("xT_ready")
        h0_made = sem("h0_made")
        h0_ready = sem("h0_ready")
        summed = sem("summed")
        h_ready = sem("h_ready")
        logits_made = sem("logits_made")
        route_step = sem("route_step")
        onehot_ready = sem("onehot_ready")
        onehotT_made = sem("onehotT_made")
        onehotT_ready = sem("onehotT_ready")
        mask_made = sem("mask_made")
        hm_ready = sem("hm_ready")
        z_made = sem("z_made")
        g_ready = sem("g_ready")
        gm_ready = sem("gm_ready")
        y_made = sem("y_made")
        y_ready = sem("y_ready")
        stored = sem("stored")

        block = ctx.enter_context(nc.Block())

        S_MASK = 5
        S_MM1 = 9
        S_MM2 = S_MM1 + KB * (E + 1) + 1
        R = 5

        def state(t):
            k = t + C
            return hT[:, k // C, :, k % C]

        def pre_of(t):
            return pre[:, t // C % 2, t % C:t % C + C + 1:C]

        @block.sync
        def _(sp):
            for b in range(B):
                sp.dma_start(x_sb[b * C:(b + 1) * C, 0, :], x[b, 0:C, :]).then_inc(x0_loaded, 16)
            sp.dma_start(Wh_sb[:, :], Wh).then_inc(wh_loaded, 16)
            for b in range(B):
                sp.dma_start(x_sb[b * C:(b + 1) * C, 1:NCH, :],
                             x[b, C:T, :].rearrange("(c s) d -> s c d", s=C)).then_inc(x_loaded, 16)
            sp.dma_start(W1_sb[:, :, :], W1.rearrange("e d h -> d e h")).then_inc(w1_loaded, 16)
            sp.dma_start(b1_sb[:, :], b1).then_inc(w1_loaded, 16)
            sp.dma_start(W2_sb[:, :, :, :].rearrange("p e k d -> p (e k) d"),
                         W2.rearrange("e (k p) d -> p (e k) d", p=128)).then_inc(w2_loaded, 16)
            sp.dma_start(b2_sb[:, :], b2).then_inc(w2_loaded, 16)
            for c in range(NCH):
                sp.wait_ge(y_ready, c + 1)
                for b in range(B):
                    sp.dma_start(out[b, c * C:(c + 1) * C, :],
                                 y_sb[b * C:(b + 1) * C, c, :]).then_inc(stored, 16)
            sp.wait_ge(stored, 16 * B * NCH)

        @block.gpsimd
        def _(pool):
            nc.gpsimd.memset(ident[:, :], 0.0).then_inc(ident_zeroed, 1)
            pool.wait_ge(ident_zeroed, 1)
            nc.gpsimd.affine_select(out=ident[:, :], in_=ident[:, :], compare_op=ALU.not_equal, fill=1.0,
                                    base=0, pattern=[[-1, 128]], channel_multiplier=1).then_inc(ident_ready, 1)
            for e in range(E):
                last = nc.gpsimd.memset(desc[:, e:e + 1], float(E - e))
            last.then_inc(desc_ready, 1)

        def hidden_gelu(act, c, k):
            act.wait_ge(z_made, KB * c + k + 1)
            nc.scalar.activation(g[:, k, :], z[:, k % 2, 0:N], ACT.Gelu).then_inc(g_ready, 1)

        @block.scalar
        def _(act):
            act.dma_start(Wx_sb[:, :], Wx).then_inc(wx_loaded, 16)
            act.dma_start(cond_sb[:, :], cond).then_inc(cond_loaded, 16)
            act.dma_start(Wr_sb[:, :], Wr).then_inc(wr_loaded, 16)
            act.dma_start(br_sb[:, :], br.rearrange("(o e) -> o e", o=1).to_broadcast([N, E])).then_inc(wr_loaded, 16)
            for t in range(T):
                c, s = divmod(t, C)
                act.wait_ge(summed, t + 1)
                nc.scalar.activation(state(t), pre_of(t), ACT.Tanh).then_inc(h_ready, 1)
                if c >= 1:
                    k, r = divmod(s - 2 - S_MM1, E + 1)
                    if r == E and 0 <= k < KB:
                        hidden_gelu(act, c - 1, k)
            for k in range(KB):
                hidden_gelu(act, NCH - 1, k)

        @block.vector
        def _(dve):
            dve.wait_ge(ident_ready, 1)
            nc.vector.tensor_copy(ident16[:, :], ident[:, :]).then_inc(ident16_ready, 1)
            for c in range(NCH):
                dve.wait_ge(xT_made, c + 1)
                nc.vector.tensor_copy(xT[:, c, :], y[:, 0:N]).then_inc(xT_ready, 1)
                if c == 0:
                    dve.wait_ge(h0_made, 1)
                    nc.vector.tensor_copy(state(-1), small[:, 2, 0:B]).then_inc(h0_ready, 1)
            dve.wait_ge(wr_loaded, 32)
            dve.wait_ge(desc_ready, 1)
            for c in range(NCH):
                dve.wait_ge(logits_made, c + 1)
                nc.vector.tensor_tensor(logit[:, :], small[:, 0, 0:E], br_sb[:, :], ALU.add).then_inc(route_step, 1)
                dve.wait_ge(route_step, 4 * c + 1)
                nc.vector.max(top[:, :], logit[:, :]).then_inc(route_step, 1)
                dve.wait_ge(route_step, 4 * c + 2)
                nc.vector.scalar_tensor_tensor(cand[:, :], logit[:, :], top[:, 0:1], desc[:, :],
                                               ALU.is_equal, ALU.mult).then_inc(route_step, 1)
                dve.wait_ge(route_step, 4 * c + 3)
                nc.vector.tensor_reduce(first[:, :], cand[:, :], AX.X, ALU.max).then_inc(route_step, 1)
                dve.wait_ge(route_step, 4 * c + 4)
                nc.vector.tensor_scalar(onehot[:, :], cand[:, :], first[:, 0:1], None,
                                        ALU.is_equal).then_inc(onehot_ready, 1)
                dve.wait_ge(onehotT_made, c + 1)
                nc.vector.tensor_copy(onehotT[:, :], small[0:E, 1, :]).then_inc(onehotT_ready, 1)
                dve.wait_ge(mask_made, c + 1)
                nc.vector.tensor_tensor(hm[:, :, :], mask[:, :, :],
                                        hT[:, c + 1:c + 2, :, :].rearrange("p o b s -> p o (b s)")
                                        .to_broadcast([D, E, N]), ALU.mult).then_inc(hm_ready, 1)
                for k in range(KB):
                    dve.wait_ge(g_ready, KB * c + k + 1)
                    nc.vector.tensor_tensor(gm[:, k, :, :], mask[:, :, :],
                                            g[:, k:k + 1, :].to_broadcast([128, E, N]), ALU.mult).then_inc(gm_ready, 1)
                dve.wait_ge(y_made, c + 1)
                nc.vector.tensor_tensor(y_sb[:, c, :], y[:, 0:D], x_sb[:, c, :], ALU.add).then_inc(y_ready, 1)

        @block.tensor
        def _(pe):
            def transpose_x(c):
                if c >= 1:
                    pe.wait_ge(xT_ready, c)
                nc.tensor.transpose(y[:, 0:N], x_sb[:, c, :], ident[:, :]).then_inc(xT_made, 1)

            def project_x(c):
                pe.wait_ge(xT_ready, c + 1)
                nc.tensor.matmul(pre[:, c % 2, 0:N], Wx_sb[:, :], xT[:, c, :], start=True, stop=True)

            def step(t):
                c, s = divmod(t, C)
                if t:
                    pe.wait_ge(h_ready, t)
                nc.tensor.matmul(pre_of(t), Wh_sb[:, :], state(t - 1), start=False, stop=True,
                                 skip_group_check=True).then_inc(summed, 1)

            def ffn_slot(c, s):
                if s == 0:
                    if c == 0:
                        pe.wait_ge(wr_loaded, 32)
                    pe.wait_ge(h_ready, C * (c + 1))
                    nc.tensor.matmul(small[0:N, 0, 0:E], hT[:, c + 1, :, :].rearrange("p b s -> p (b s)"),
                                     Wr_sb[:, :], start=True, stop=True).then_inc(logits_made, 1)
                elif s == S_MASK:
                    pe.wait_ge(onehot_ready, c + 1)
                    nc.tensor.matmul(small[0:E, 1, :], onehot[:, :], ident16[:, :], start=True, stop=True)\
                      .then_inc(onehotT_made, 1)
                    for e in range(E // 2):
                        nc.tensor.matmul(mask[:, e, :], onehot[:, e:e + 1].to_broadcast([N, 128]), ident16[:, :],
                                         start=True, stop=True)
                elif s == S_MASK + 1:
                    for e in range(E // 2, E):
                        last = nc.tensor.matmul(mask[:, e, :], onehot[:, e:e + 1].to_broadcast([N, 128]),
                                                ident16[:, :], start=True, stop=True)
                    last.then_inc(mask_made, 1)
                elif S_MM1 <= s < S_MM1 + KB * (E + 1):
                    k, e = divmod(s - S_MM1, E + 1)
                    if c == 0 and k == 0 and e == 0:
                        pe.wait_ge(w1_loaded, 32)
                    if e < E:
                        if k == 0 and e == 0:
                            pe.wait_ge(hm_ready, c + 1)
                        elif k >= 2 and e == 0:
                            pe.wait_ge(g_ready, KB * c + k - 1)
                        nc.tensor.matmul(z[:, k % 2, 0:N], W1_sb[:, e, k * 128:(k + 1) * 128], hm[:, e, :],
                                         start=(e == 0), stop=False)
                    else:
                        if k == 0:
                            pe.wait_ge(onehotT_ready, c + 1)
                        nc.tensor.matmul(z[:, k % 2, 0:N], b1_sb[:, k * 128:(k + 1) * 128], onehotT[:, :],
                                         start=False, stop=True).then_inc(z_made, 1)
                elif S_MM2 <= s < S_MM2 + 1 + KB * E:
                    k, e = divmod(s - S_MM2, E)
                    if c == 0 and k == 0 and e == 0:
                        pe.wait_ge(w2_loaded, 32)
                    if k < KB:
                        if e == 0:
                            pe.wait_ge(gm_ready, KB * c + k + 1)
                        nc.tensor.matmul(y[:, 0:D], gm[:, k, e, :], W2_sb[:, e, k, :],
                                         start=(k == 0 and e == 0), stop=False)
                    else:
                        nc.tensor.matmul(y[:, 0:D], onehotT[:, :], b2_sb[:, :], start=False, stop=True)\
                          .then_inc(y_made, 1)

            pe.wait_ge(ident_ready, 1)
            pe.wait_ge(x0_loaded, 16 * B)
            transpose_x(0)
            pe.wait_ge(cond_loaded, 16)
            nc.tensor.transpose(small[:, 2, 0:B], cond_sb[:, :], ident[0:B, 0:B]).then_inc(h0_made, 1)
            pe.wait_ge(wx_loaded, 16)
            project_x(0)
            pe.wait_ge(wh_loaded, 16)
            pe.wait_ge(h0_ready, 1)
            for c in range(NCH):
                for s in range(C):
                    step(c * C + s)
                    if c == 0:
                        j, r = divmod(s - 12, 6)
                        if 0 <= j < NCH - 1:
                            if r == 0:
                                if j == 0:
                                    pe.wait_ge(x_loaded, 16 * B)
                                transpose_x(j + 1)
                        if s == C - 1:
                            pe.wait_ge(ident16_ready, 1)
                    else:
                        ffn_slot(c - 1, s)
                    if s == C - 2 and c + 1 < NCH:
                        project_x(c + 1)
            for s in range(C):
                ffn_slot(NCH - 1, s)


_INS = ["x", "cond_1024", "L0_cond_Wx", "L0_cond_Wh", "L0_ffn_Wr", "L0_ffn_br", "L0_ffn_W1", "L0_ffn_b1",
        "L0_ffn_W2", "L0_ffn_b2"]
_OUTS = [((B, T, D), "float32")]


def kernel(**inputs):
    import numpy as _np
    import concourse.bacc as _bacc
    from concourse import mybir as _mybir
    from concourse.bass_utils import run_bass_kernel_spmd as _run

    nc = _bacc.Bacc("TRN2", target_bir_lowering=False, num_devices=1)
    arrays, args = {}, []
    for name in _INS:
        a = _np.ascontiguousarray(inputs[name])
        arrays[f"in_{name}_dram"] = a
        args.append(nc.dram_tensor(f"in_{name}_dram", a.shape, _mybir.dt.from_np(a.dtype), kind="ExternalInput").ap())
    for i, (shape, dtype) in enumerate(_OUTS):
        dt = _mybir.dt.from_np(_np.dtype(dtype))
        args.append(nc.dram_tensor(f"out_{i}_dram", shape, dt, kind="ExternalOutput").ap())
    build(nc, *args)
    r = _run(nc, [arrays], core_ids=[0])
    got = tuple(r.results[0][f"out_{i}_dram"] for i in range(len(_OUTS)))
    return got[0]
```

```python
import concourse.bass as bass
from concourse import mybir
from concourse.alu_op_type import AluOpType as ALU
from contextlib import ExitStack

F32 = mybir.dt.float32
BF16 = mybir.dt.bfloat16
F16 = mybir.dt.float16
ACT = mybir.ActivationFunctionType

B, T, D = 2, 512, 128
E, H = 8, 384
KB = H // 128
C = 32
N = B * C
NCH = T // C

UP = 2.0 ** 10

S_MASK = 2
S_HM = S_MASK + 2
S_MM = S_HM + 3
ROOM = 8
MM1 = KB * E + KB
MM2 = KB * E + 1


def passes_before(n):
    return 4 * n - 3 * min(n // (E + 1), KB)


def slot_of(n):
    return S_MM + passes_before(n) // ROOM


S_GELU = [slot_of((k + 1) * (E + 1) - 1) + 1 for k in range(KB)]
S_TURN, S_STORE = 1, 2
S_XT, S_XP = 3, (4, 5)
S_XT0, S_XP0 = C - 6, (C - 4, C - 3)
S_W1 = 5
assert S_W1 + 3 * E + 1 < C
assert slot_of(MM1 + MM2 - 1) < C
assert S_GELU[KB - 1] + 2 < slot_of(MM1 + (KB - 1) * E)


def build(nc, x, cond, Wx, Wh, Wr, br, W1, b1, W2, b2, out):
    ctx = ExitStack()
    with ctx:
        def sb(name, shape, dt=F32):
            return ctx.enter_context(nc.sbuf_tensor(name, shape, dt))

        def ps(name, shape, dt=F32):
            return ctx.enter_context(nc.psum_tensor(name, shape, dt))

        def sem(name):
            return ctx.enter_context(nc.semaphore(name))

        x_sb = sb("x_sb", [N, NCH, D])
        cond_sb = sb("cond_sb", [B, D])
        Wx_sb = sb("Wx_sb", [D, D])
        Wh_sb = sb("Wh_sb", [D, D])
        Wr_sb = sb("Wr_sb", [D, E])
        br_sb = sb("br_sb", [N, E])
        W1_sb = sb("W1_sb", [D, E, H])
        W2_sb = sb("W2_sb", [128, E, KB, D])
        b_sb = sb("b_sb", [128, H + D])
        Wh_up = sb("Wh_up", [D, D])
        Wh_rest = sb("Wh_rest", [D, D])
        Wh_part = sb("Wh_part", [D, 3, D], BF16)
        Wh_16 = sb("Wh_16", [D, D], F16)
        Wr_up = sb("Wr_up", [D, E])
        Wr_rest = sb("Wr_rest", [D, E])
        Wr_part = sb("Wr_part", [D, 3, E], BF16)
        Wr_16 = sb("Wr_16", [D, E], F16)
        br_up = sb("br_up", [N, E])
        W1_rest = sb("W1_rest", [D, E, H])
        W1_part = sb("W1_part", [D, 3, E, H], BF16)
        W1_16 = sb("W1_16", [D, E, H], F16)
        W2_rest = sb("W2_rest", [128, E, KB, D])
        W2_part = sb("W2_part", [128, 3, E, KB, D], BF16)
        W2_16 = sb("W2_16", [128, E, KB, D], F16)
        b_rest = sb("b_rest", [128, H + D])
        b_part = sb("b_part", [128, H + D], BF16)
        ident = sb("ident", [128, 128])
        ident16 = sb("ident16", [128, 128], BF16)
        desc = sb("desc", [N, E])
        x_stage = sb("x_stage", [N, 2, D])
        xT = sb("xT", [D, 2, N])
        h0_up = sb("h0_up", [D, B])
        hi = sb("hi", [D, 2, B, C], F16)
        lo = sb("lo", [D, 2, B, C], F16)
        extreme = sb("extreme", [128, 1 + KB])
        logit = sb("logit", [N, E])
        top = sb("top", [N, 1])
        cand = sb("cand", [N, E])
        first = sb("first", [N, 1])
        onehot = sb("onehot", [128, 4, 32], BF16)
        onehotT = sb("onehotT", [128, N], BF16)
        mask_up = sb("mask_up", [128, E, N], F16)
        mask_one = sb("mask_one", [128, E, N], F16)
        hm_hi = sb("hm_hi", [D, E, N], F16)
        hm_lo = sb("hm_lo", [D, E, N], F16)
        g = sb("g", [128, KB, N])
        g_hi = sb("g_hi", [128, KB, N], F16)
        g_lo = sb("g_lo", [128, KB, N], F16)
        gm_hi = sb("gm_hi", [128, KB, E, N], F16)
        gm_lo = sb("gm_lo", [128, KB, E, N], F16)
        yT = sb("yT", [D, N])
        y_sb = sb("y_sb", [N, 2, D])
        pre = ps("pre", [128, 2, 512])
        state = ps("state", [128, 256, B])
        mask = ps("mask", [128, E, N])
        z = ps("z", [128, 2, 512])
        y = ps("y", [128, 4, 128])
        small = ps("small", [128, 4, 128])

        x0_loaded = sem("x0_loaded")
        x_loaded = sem("x_loaded")
        cond_loaded = sem("cond_loaded")
        wx_loaded = sem("wx_loaded")
        wh_loaded = sem("wh_loaded")
        wr_loaded = sem("wr_loaded")
        w1_loaded = sem("w1_loaded")
        w2_loaded = sem("w2_loaded")
        w2_first_loaded = sem("w2_first_loaded")
        b_loaded = sem("b_loaded")
        ident_zeroed = sem("ident_zeroed")
        ident_ready = sem("ident_ready")
        ident16_ready = sem("ident16_ready")
        desc_ready = sem("desc_ready")
        pads_zeroed = sem("pads_zeroed")
        x_staged = sem("x_staged")
        xT_made = sem("xT_made")
        xT_ready = sem("xT_ready")
        projected = sem("projected")
        h0_made = sem("h0_made")
        h0_ready = sem("h0_ready")
        wh_up_ready = sem("wh_up_ready")
        wh_split = sem("wh_split")
        wh_16_ready = sem("wh_16_ready")
        wr_split = sem("wr_split")
        b_split = sem("b_split")
        w1_cast = sem("w1_cast")
        w1_rest = sem("w1_rest")
        w2_split = sem("w2_split")
        summed = sem("summed")
        h_ready = sem("h_ready")
        lo_ready = sem("lo_ready")
        logits_made = sem("logits_made")
        route_step = sem("route_step")
        onehot_ready = sem("onehot_ready")
        onehotT_made = sem("onehotT_made")
        onehotT_ready = sem("onehotT_ready")
        mask_made = sem("mask_made")
        mask_up_ready = sem("mask_up_ready")
        mask_one_ready = sem("mask_one_ready")
        hm_ready = sem("hm_ready")
        z_made = sem("z_made")
        g_ready = sem("g_ready")
        g_lo_ready = sem("g_lo_ready")
        gm_ready = sem("gm_ready")
        y_made = sem("y_made")
        yT_ready = sem("yT_ready")
        y_turned = sem("y_turned")
        y_ready = sem("y_ready")
        stored = [sem(f"stored_{q}") for q in range(2)]

        block = ctx.enter_context(nc.Block())

        def columns(buf, q, s):
            if buf is pre:
                return pre[:, q, s:s + C + 1:C]
            return buf[:, q, :, s]

        def before(q, s):
            return (q, s - 1) if s else (1 - q, C - 1)

        @block.sync
        def _(sp):
            sp.dma_start(x_sb[0:C, 0, :], x[0, 0:C, :]).then_inc(x0_loaded, 16)
            sp.dma_start(Wx_sb[:, :], Wx).then_inc(wx_loaded, 16)
            sp.dma_start(W1_sb[:, :, :], W1.rearrange("e d h -> d e h")).then_inc(w1_loaded, 16)
            for b in range(B):
                sp.dma_start(x_sb[b * C:(b + 1) * C, 1:NCH, :],
                             x[b, C:T, :].rearrange("(c s) d -> s c d", s=C)).then_inc(x_loaded, 16)
            sp.dma_start(W2_sb[:, :, :, :].rearrange("p e k d -> p (e k) d"),
                         W2.rearrange("e (k p) d -> p (e k) d", p=128)).then_inc(w2_loaded, 16)

            def store(c, q):
                sp.wait_ge(y_ready, c + 1)
                for b in range(B):
                    sp.dma_start(out[b, c * C:(c + 1) * C, :],
                                 y_sb[b * C:(b + 1) * C, q, :]).then_inc(stored[q], 16)

            for c in range(NCH):
                store(c, c % 2)
            for q in range(2):
                sp.wait_ge(stored[q], 16 * B * (NCH // 2))

        @block.gpsimd
        def _(pool):
            def stage_x(c, q):
                if c >= 2:
                    pool.wait_ge(xT_made, c - 1)
                nc.gpsimd.tensor_copy(x_stage[:, q, :], x_sb[:, c, :]).then_inc(x_staged, 1)

            def split_w2(k):
                w, rest = W2_sb[:, :, k, :], W2_rest[:, :, k, :]
                nc.gpsimd.tensor_tensor(rest, w, W2_part[:, 0, :, k, :], ALU.subtract).then_inc(w2_split, 1)
                nc.gpsimd.tensor_copy(W2_16[:, :, k, :], w).then_inc(w2_split, 1)
                pool.wait_ge(w2_split, 4 * k + 1)
                nc.gpsimd.tensor_copy(W2_part[:, 1, :, k, :], rest).then_inc(w2_split, 1)
                pool.wait_ge(w2_split, 4 * k + 3)
                nc.gpsimd.tensor_tensor(W2_part[:, 2, :, k, :], rest, W2_part[:, 1, :, k, :], ALU.subtract)\
                  .then_inc(w2_split, 1)

            pool.dma_start(cond_sb[:, :], cond).then_inc(cond_loaded, 16)
            nc.gpsimd.memset(ident[:, :], 0.0).then_inc(ident_zeroed, 1)
            nc.gpsimd.memset(b_sb[:, :], 0.0).then_inc(pads_zeroed, 1)
            nc.gpsimd.memset(onehot[:, :, :], 0.0).then_inc(pads_zeroed, 1)
            pool.wait_ge(ident_zeroed, 1)
            nc.gpsimd.affine_select(out=ident[:, :], in_=ident[:, :], compare_op=ALU.not_equal, fill=1.0,
                                    base=0, pattern=[[-1, 128]], channel_multiplier=1).then_inc(ident_ready, 1)
            for e in range(E):
                last = nc.gpsimd.memset(desc[:, e:e + 1], float(E - e))
            last.then_inc(desc_ready, 1)
            pool.dma_start(Wr_sb[:, :], Wr).then_inc(wr_loaded, 16)
            pool.dma_start(br_sb[:, :], br.rearrange("(o e) -> o e", o=1).to_broadcast([N, E])).then_inc(wr_loaded, 16)
            pool.wait_ge(pads_zeroed, 2)
            for i in range(3):
                pool.dma_start(b_sb[32 * i:32 * i + E, 0:H], b1).then_inc(b_loaded, 16)
                pool.dma_start(b_sb[32 * i:32 * i + E, H:H + D], b2).then_inc(b_loaded, 16)
            pool.dma_start(W2_part[:, 0, :, :, :].rearrange("p e k d -> p (e k) d"),
                           W2.rearrange("e (k p) d -> p (e k) d", p=128)).then_inc(w2_first_loaded, 16)
            pool.wait_ge(x_loaded, 16 * B)
            stage_x(1, 1)
            pool.wait_ge(w2_loaded, 16)
            pool.wait_ge(w2_first_loaded, 16)
            split_w2(0)
            stage_x(2, 0)
            split_w2(1)
            stage_x(3, 1)
            split_w2(2)
            for c in range(4, NCH):
                stage_x(c, c % 2)

        @block.scalar
        def _(act):
            def step(t, q, s):
                act.wait_ge(summed, t + 1)
                nc.scalar.activation(columns(hi, q, s), columns(pre, q, s), ACT.Tanh, scale=1 / UP)
                nc.scalar.activation(state[:, 0, :], columns(pre, q, s), ACT.Tanh, scale=1 / UP).then_inc(h_ready, 1)

            def ffn_slot(c, s):
                if s == 0 and c > 0:
                    take_y(c - 1)
                if s == S_MASK + 1:
                    act.wait_ge(mask_made, c + 1)
                    nc.scalar.mul(mask_up[:, :, :], mask[:, :, :], UP).then_inc(mask_up_ready, 1)
                for k in range(KB):
                    if s == S_GELU[k]:
                        act.wait_ge(z_made, KB * c + k + 1)
                        nc.scalar.activation(g_hi[:, k, :], z[:, k % 2, 0:N], ACT.Gelu, scale=1 / UP)
                        nc.scalar.activation(g[:, k, :], z[:, k % 2, 0:N], ACT.Gelu, scale=1 / UP)\
                          .then_inc(g_ready, 1)

            def take_y(c):
                act.wait_ge(y_made, c + 1)
                nc.scalar.mul(yT[:, :], y[:, 0, 0:N], 1 / UP).then_inc(yT_ready, 1)

            def cast_w1(e, i):
                if i == 0:
                    nc.scalar.copy(W1_part[:, 0, e, :], W1_sb[:, e, :]).then_inc(w1_cast, 1)
                elif i == 1:
                    nc.scalar.copy(W1_16[:, e, :], W1_sb[:, e, :]).then_inc(w1_cast, 1)
                else:
                    act.wait_ge(w1_rest, 2 * e + 1)
                    nc.scalar.copy(W1_part[:, 1, e, :], W1_rest[:, e, :]).then_inc(w1_cast, 1)

            act.dma_start(x_sb[C:2 * C, 0, :], x[1, 0:C, :]).then_inc(x0_loaded, 16)
            act.dma_start(Wh_sb[:, :], Wh).then_inc(wh_loaded, 16)
            act.wait_ge(ident_ready, 1)
            nc.scalar.activation(yT[:, 0:1], ident[:, 0:1], ACT.Gelu)
            act.wait_ge(wh_loaded, 16)
            nc.scalar.copy(Wh_16[:, :], Wh_sb[:, :]).then_inc(wh_16_ready, 1)
            for c in range(NCH):
                for s in range(C):
                    step(c * C + s, c % 2, s)
                    if c == 0:
                        e, i = divmod(s - S_W1, 3)
                        if 0 <= e < E:
                            if e == 0 and i == 0:
                                act.wait_ge(w1_loaded, 16)
                            cast_w1(e, i)
                    else:
                        ffn_slot(c - 1, s)
            for s in range(C):
                ffn_slot(NCH - 1, s)
            take_y(NCH - 1)

        @block.vector
        def _(dve):
            def low_part(out, v, v_hi, by_product):
                return nc.vector.tensor_tensor_reduce(out=out, in0=v, in1=v_hi, scale=UP, scalar=0.0,
                                                      op0=ALU.subtract, op1=ALU.max, accum_out=extreme[:, by_product:by_product + 1])

            def split_state(t, q, s):
                dve.wait_ge(h_ready, t + 1)
                low_part(columns(lo, q, s), state[:, 0, :], columns(hi, q, s), 0).then_inc(lo_ready, 1)

            def ffn_slot(c, q, s):
                chunk_hi = hi[:, q:q + 1, :, :].rearrange("p o b s -> p o (b s)").to_broadcast([D, E, N])
                chunk_lo = lo[:, q:q + 1, :, :].rearrange("p o b s -> p o (b s)").to_broadcast([D, E, N])
                if s == 0:
                    dve.wait_ge(logits_made, c + 1)
                    nc.vector.tensor_tensor_reduce(out=logit[:, :], in0=small[0:N, 0, 0:E], in1=br_up[:, :],
                                                   scale=1.0, scalar=-3.0e38, op0=ALU.add, op1=ALU.max,
                                                   accum_out=top[:, :]).then_inc(route_step, 1)
                    dve.wait_ge(route_step, 3 * c + 1)
                    nc.vector.scalar_tensor_tensor(cand[:, :], logit[:, :], top[:, 0:1], desc[:, :],
                                                   ALU.is_equal, ALU.mult).then_inc(route_step, 1)
                    dve.wait_ge(route_step, 3 * c + 2)
                    nc.vector.tensor_reduce(first[:, :], cand[:, :], mybir.AxisListType.X, ALU.max)\
                      .then_inc(route_step, 1)
                elif s == 1:
                    dve.wait_ge(route_step, 3 * c + 3)
                    nc.vector.tensor_scalar(onehot[0:N, 0:3, 0:E],
                                            cand[:, :].rearrange("p (o e) -> p o e", o=1).to_broadcast([N, 3, E]),
                                            first[:, 0:1], None, ALU.is_equal).then_inc(onehot_ready, 1)
                if s == S_STORE and c > 0:
                    add_residual(c - 1, 1 - q)
                if s == S_HM:
                    dve.wait_ge(mask_up_ready, c + 1)
                    nc.vector.tensor_tensor(hm_hi[:, :, :], mask_up[:, :, :], chunk_hi, ALU.mult).then_inc(hm_ready, 1)
                    nc.vector.tensor_scalar(mask_one[:, :, :], mask_up[:, :, :], 1 / UP, None, ALU.mult)\
                      .then_inc(mask_one_ready, 1)
                elif s == S_HM + 1:
                    dve.wait_ge(mask_one_ready, c + 1)
                    nc.vector.tensor_tensor(hm_lo[:, :, :], mask_one[:, :, :], chunk_lo, ALU.mult).then_inc(hm_ready, 1)
                elif s == S_HM + 2:
                    dve.wait_ge(onehotT_made, c + 1)
                    nc.vector.tensor_scalar(onehotT[:, :], small[:, 1, 0:N], UP, None, ALU.mult)\
                      .then_inc(onehotT_ready, 1)
                for k in range(KB):
                    if s == S_GELU[k]:
                        dve.wait_ge(g_ready, KB * c + k + 1)
                        low_part(g_lo[:, k, :], g[:, k, :], g_hi[:, k, :], 1 + k).then_inc(g_lo_ready, 1)
                    elif s == S_GELU[k] + 1:
                        nc.vector.tensor_tensor(gm_hi[:, k, :, :], mask_up[:, :, :],
                                                g_hi[:, k:k + 1, :].to_broadcast([128, E, N]), ALU.mult)\
                          .then_inc(gm_ready, 1)
                    elif s == S_GELU[k] + 2:
                        dve.wait_ge(g_lo_ready, KB * c + k + 1)
                        nc.vector.tensor_tensor(gm_lo[:, k, :, :], mask_one[:, :, :],
                                                g_lo[:, k:k + 1, :].to_broadcast([128, E, N]), ALU.mult)\
                          .then_inc(gm_ready, 1)

            def add_residual(c, q):
                dve.wait_ge(y_turned, c + 1)
                if c >= 2:
                    dve.wait_ge(stored[q], 16 * B * (c // 2))
                nc.vector.tensor_tensor(y_sb[:, q, :], y[0:N, 1, :], x_sb[:, c, :], ALU.add).then_inc(y_ready, 1)

            def take_xT(c, q):
                dve.wait_ge(xT_made, c + 1)
                nc.vector.tensor_scalar(xT[:, q, :], y[:, 2, 0:N], UP, None, ALU.mult).then_inc(xT_ready, 1)

            def split_w1(e, i):
                if i == 1:
                    dve.wait_ge(w1_cast, 3 * e + 1)
                    nc.vector.tensor_tensor(W1_rest[:, e, :], W1_sb[:, e, :], W1_part[:, 0, e, :], ALU.subtract)\
                      .then_inc(w1_rest, 1)
                elif i == 3:
                    dve.wait_ge(w1_cast, 3 * e + 3)
                    nc.vector.tensor_tensor(W1_part[:, 2, e, :], W1_rest[:, e, :], W1_part[:, 1, e, :], ALU.subtract)\
                      .then_inc(w1_rest, 1)

            dve.wait_ge(ident_ready, 1)
            nc.vector.tensor_copy(ident16[:, :], ident[:, :]).then_inc(ident16_ready, 1)
            take_xT(0, 0)
            dve.wait_ge(h0_made, 1)
            nc.vector.tensor_scalar(h0_up[:, :], y[:, 3, 0:B], UP, None, ALU.mult).then_inc(h0_ready, 1)

            def split(w, rest, part, done, count):
                nc.vector.tensor_scalar(part[0], w, UP, None, ALU.mult).then_inc(done, 1)
                dve.wait_ge(done, count + 1)
                nc.vector.scalar_tensor_tensor(rest, w, UP, part[0], ALU.mult, ALU.subtract).then_inc(done, 1)
                dve.wait_ge(done, count + 2)
                nc.vector.tensor_copy(part[1], rest).then_inc(done, 1)
                dve.wait_ge(done, count + 3)
                nc.vector.tensor_tensor(part[2], rest, part[1], ALU.subtract).then_inc(done, 1)

            dve.wait_ge(pads_zeroed, 2)
            dve.wait_ge(desc_ready, 1)
            dve.wait_ge(wh_loaded, 16)
            split(Wh_sb[:, :], Wh_rest[:, :], [Wh_part[:, i, :] for i in range(3)], wh_split, 0)

            def first_chunk_slot(s):
                if s == 1:
                    dve.wait_ge(wr_loaded, 32)
                    nc.vector.tensor_scalar(Wr_part[:, 0, :], Wr_sb[:, :], UP, None, ALU.mult).then_inc(wr_split, 1)
                    nc.vector.tensor_scalar(br_up[:, :], br_sb[:, :], UP, None, ALU.mult).then_inc(wr_split, 1)
                    nc.vector.tensor_copy(Wr_16[:, :], Wr_sb[:, :]).then_inc(wr_split, 1)
                elif s == 2:
                    dve.wait_ge(wr_split, 1)
                    nc.vector.scalar_tensor_tensor(Wr_rest[:, :], Wr_sb[:, :], UP, Wr_part[:, 0, :],
                                                   ALU.mult, ALU.subtract).then_inc(wr_split, 1)
                    dve.wait_ge(wr_split, 4)
                    nc.vector.tensor_copy(Wr_part[:, 1, :], Wr_rest[:, :]).then_inc(wr_split, 1)
                elif s == 5:
                    dve.wait_ge(wr_split, 5)
                    nc.vector.tensor_tensor(Wr_part[:, 2, :], Wr_rest[:, :], Wr_part[:, 1, :], ALU.subtract)\
                      .then_inc(wr_split, 1)
                elif s == 7:
                    dve.wait_ge(b_loaded, 16 * 6)
                    nc.vector.tensor_copy(b_part[:, :], b_sb[:, :]).then_inc(b_split, 1)
                elif s == 10:
                    dve.wait_ge(b_split, 1)
                    nc.vector.tensor_tensor(b_rest[:, 0:H], b_sb[:, 0:H], b_part[:, 0:H], ALU.subtract)\
                      .then_inc(b_split, 1)
                elif s == 13:
                    nc.vector.tensor_tensor(b_rest[:, H:H + D], b_sb[:, H:H + D], b_part[:, H:H + D],
                                            ALU.subtract).then_inc(b_split, 1)
                elif s in (16, 19):
                    i = 1 if s == 16 else 2
                    dve.wait_ge(b_split, 3)
                    nc.vector.tensor_copy(b_part[32 * i:32 * i + 32, :], b_rest[32 * i:32 * i + 32, :])\
                      .then_inc(b_split, 1)
                elif s == 22:
                    dve.wait_ge(b_split, 5)
                    nc.vector.tensor_tensor(b_part[64:96, :], b_rest[64:96, :], b_part[64:96, :], ALU.subtract)\
                      .then_inc(b_split, 1)

            for c in range(NCH):
                for s in range(C):
                    split_state(c * C + s, c % 2, s)
                    if c == 0:
                        for e in range(E):
                            split_w1(e, s - S_W1 - 3 * e)
                        first_chunk_slot(s)
                    else:
                        ffn_slot(c - 1, 1 - c % 2, s)
                    if s == (S_XT if c else S_XT0) and c + 1 < NCH:
                        take_xT(c + 1, 1 - c % 2)
            for s in range(C):
                ffn_slot(NCH - 1, 1, s)
            add_residual(NCH - 1, 1)

        @block.tensor
        def _(pe):
            def transpose_x(c, q):
                if c == 0:
                    nc.tensor.transpose(y[:, 2, 0:N], x_sb[:, 0, :], ident[0:N, 0:N]).then_inc(xT_made, 1)
                else:
                    pe.wait_ge(x_staged, c)
                    nc.tensor.transpose(y[:, 2, 0:N], x_stage[:, q, :], ident[0:N, 0:N]).then_inc(xT_made, 1)

            def project_x(c, q, half):
                if half == 0:
                    pe.wait_ge(xT_ready, c + 1)
                own = slice(half * D // 2, (half + 1) * D // 2)
                nc.tensor.matmul(pre[own, q, 0:N], Wx_sb[:, own], xT[:, q, :], start=True, stop=True)

            def add(out, parts, v_hi, w_16, v_lo, start, stop):
                for i in (0, 1, 2):
                    nc.tensor.matmul(out, parts[i], v_hi, start=start and i == 0, stop=False)
                return nc.tensor.matmul(out, w_16, v_lo, start=False, stop=stop)

            def step(t, q, s):
                def add_state(part, state_part):
                    return nc.tensor.matmul(columns(pre, q, s), part, state_part, start=False, stop=True,
                                            skip_group_check=True)

                pe.wait_ge(h_ready, t)
                for i in (2, 1, 0):
                    add_state(Wh_part[:, i, :], columns(hi, *before(q, s)))
                pe.wait_ge(lo_ready, t)
                add_state(Wh_16[:, :], columns(lo, *before(q, s))).then_inc(summed, 1)

            def product(c, n):
                if n < MM1:
                    k, e = divmod(n, E + 1)
                    if e == 0 and k == 0:
                        pe.wait_ge(hm_ready, 2 * (c + 1))
                    elif e == 0 and k >= 2:
                        pe.wait_ge(g_ready, KB * c + k - 1)
                    if e < E:
                        cols = slice(k * 128, (k + 1) * 128)
                        add(z[:, k % 2, 0:N], [W1_part[:, i, e, cols] for i in range(3)], hm_hi[:, e, :],
                            W1_16[:, e, cols], hm_lo[:, e, :], start=(e == 0), stop=False)
                    else:
                        if k == 0:
                            pe.wait_ge(onehotT_ready, c + 1)
                        nc.tensor.matmul(z[:, k % 2, 0:N], b_part[:, k * 128:(k + 1) * 128], onehotT[:, :],
                                         start=False, stop=True).then_inc(z_made, 1)
                else:
                    k, e = divmod(n - MM1, E)
                    if k < KB:
                        if e == 0:
                            pe.wait_ge(gm_ready, 2 * (KB * c + k + 1))
                        add(y[:, 0, 0:N], [W2_part[:, i, e, k, :] for i in range(3)], gm_hi[:, k, e, :],
                            W2_16[:, e, k, :], gm_lo[:, k, e, :], start=(k == 0 and e == 0), stop=False)
                    else:
                        nc.tensor.matmul(y[:, 0, 0:N], b_part[:, H:H + D], onehotT[:, :], start=False, stop=True)\
                          .then_inc(y_made, 1)

            def turn_y(c):
                pe.wait_ge(yT_ready, c + 1)
                nc.tensor.transpose(y[0:N, 1, :], yT[:, :], ident[:, :]).then_inc(y_turned, 1)

            def ffn_slot(c, q, s):
                if s == 0:
                    chunk_hi = hi[:, q, :, :].rearrange("p b s -> p (b s)")
                    chunk_lo = lo[:, q, :, :].rearrange("p b s -> p (b s)")
                    for i in range(3):
                        nc.tensor.matmul(small[0:N, 0, 0:E], chunk_hi, Wr_part[:, i, :], start=(i == 0), stop=False)
                    nc.tensor.matmul(small[0:N, 0, 0:E], chunk_lo, Wr_16[:, :], start=False, stop=True)\
                      .then_inc(logits_made, 1)
                if s == S_TURN and c > 0:
                    turn_y(c - 1)
                if s == S_MASK:
                    pe.wait_ge(onehot_ready, c + 1)
                    for e in range(E):
                        last = nc.tensor.matmul(mask[:, e, :], onehot[:, 0, e:e + 1].to_broadcast([128, 128]),
                                                ident16[:, 0:N], start=True, stop=True)
                    last.then_inc(mask_made, 1)
                elif s == S_MASK + 1:
                    nc.tensor.matmul(small[:, 1, 0:N], onehot[:, :, :].rearrange("p i e -> p (i e)"),
                                     ident16[:, 0:N], start=True, stop=True).then_inc(onehotT_made, 1)
                elif s >= S_MM:
                    for n in range(MM1 + MM2):
                        if slot_of(n) != s:
                            continue
                        if c == 0 and n == 0:
                            pe.wait_ge(w1_cast, 3 * E)
                            pe.wait_ge(w1_rest, 2 * E)
                            pe.wait_ge(b_split, 6)
                        if c == 0 and n >= MM1 and (n - MM1) % E == 0 and (n - MM1) // E < KB:
                            pe.wait_ge(w2_split, 4 * ((n - MM1) // E + 1))
                        product(c, n)

            pe.wait_ge(ident_ready, 1)
            pe.wait_ge(x0_loaded, 16 * B)
            transpose_x(0, 0)
            pe.wait_ge(cond_loaded, 16)
            pe.wait_ge(xT_ready, 1)
            nc.tensor.transpose(y[:, 3, 0:B], cond_sb[:, :], ident[0:B, 0:B]).then_inc(h0_made, 1)
            pe.wait_ge(wx_loaded, 16)
            project_x(0, 0, 0)
            project_x(0, 0, 1)
            pe.wait_ge(wh_loaded, 16)
            pe.wait_ge(h0_ready, 1)
            nc.tensor.matmul(columns(pre, 0, 0), Wh_sb[:, :], h0_up[:, :], start=False, stop=True,
                             skip_group_check=True).then_inc(summed, 1)
            pe.wait_ge(wh_split, 4)
            pe.wait_ge(wh_16_ready, 1)
            for c in range(NCH):
                for s in range(C):
                    if c + s:
                        step(c * C + s, c % 2, s)
                    if c == 1 and s == 0:
                        pe.wait_ge(wr_split, 6)
                        pe.wait_ge(ident16_ready, 1)
                    if c >= 1:
                        ffn_slot(c - 1, 1 - c % 2, s)
                    if c + 1 < NCH:
                        if s == (S_XT if c else S_XT0):
                            if c >= 2:
                                pe.wait_ge(y_ready, c - 1)
                            transpose_x(c + 1, 1 - c % 2)
                        elif s in (S_XP if c else S_XP0):
                            project_x(c + 1, 1 - c % 2, (S_XP if c else S_XP0).index(s))
            pe.wait_ge(lo_ready, T)
            for s in range(C):
                ffn_slot(NCH - 1, 1, s)
            turn_y(NCH - 1)


_INS = ["x", "cond_1024", "L0_cond_Wx", "L0_cond_Wh", "L0_ffn_Wr", "L0_ffn_br", "L0_ffn_W1", "L0_ffn_b1",
        "L0_ffn_W2", "L0_ffn_b2"]
_OUTS = [((B, T, D), "float32")]


def kernel(**inputs):
    import numpy as _np
    import concourse.bacc as _bacc
    from concourse import mybir as _mybir
    from concourse.bass_utils import run_bass_kernel_spmd as _run

    nc = _bacc.Bacc("TRN2", target_bir_lowering=False, num_devices=1)
    arrays, args = {}, []
    for name in _INS:
        a = _np.ascontiguousarray(inputs[name])
        arrays[f"in_{name}_dram"] = a
        args.append(nc.dram_tensor(f"in_{name}_dram", a.shape, _mybir.dt.from_np(a.dtype), kind="ExternalInput").ap())
    for i, (shape, dtype) in enumerate(_OUTS):
        dt = _mybir.dt.from_np(_np.dtype(dtype))
        args.append(nc.dram_tensor(f"out_{i}_dram", shape, dt, kind="ExternalOutput").ap())
    build(nc, *args)
    r = _run(nc, [arrays], core_ids=[0])
    got = tuple(r.results[0][f"out_{i}_dram"] for i in range(len(_OUTS)))
    return got[0]
```

```python
import concourse.bass as bass
from concourse import mybir
from concourse.alu_op_type import AluOpType as ALU
from contextlib import ExitStack

F32 = mybir.dt.float32
BF16 = mybir.dt.bfloat16
F16 = mybir.dt.float16
ACT = mybir.ActivationFunctionType

B, T, D = 2, 512, 128
E, H = 8, 384
KB = H // 128
C = 32
N = B * C
NCH = T // C

UP = 2.0 ** 10

S_MASK = 2
S_HM = S_MASK + 2
S_MM = S_HM + 3
ROOM = 8

BIAS = (None, None)
PASSES = [(layer, k, *what) for layer in range(2) for k in range(KB)
          for what in [(e, part) for part in range(4) for e in range(E)] + [BIAS] * (layer == 0 or k == KB - 1)]


def passes_behind(s):
    return PASSES[max(0, (s - S_MM) * ROOM):max(0, (s - S_MM + 1) * ROOM)]


def slot_of(which):
    return S_MM + PASSES.index(which) // ROOM


def columns_behind(s):
    return {S_TURN: 100, S_MASK: SLOT_COLUMNS, S_XT: 100, S_XP[0]: 160, S_XP[1]: 160}.get(s, N * len(passes_behind(s)))


S_GELU = [slot_of((0, k, *BIAS)) + 1 for k in range(KB)]
S_TURN, S_STORE = 1, 2
S_XT, S_XP = 3, (4, 5)
S_XT0, S_XP0 = C - 6, (C - 3, C - 2)
S_W1 = 6
B_STEPS = [S_W1 + 5 + 3 * i for i in range(6)]
assert S_W1 + 3 * E < C

GAP_COLUMNS = 112
SLOT_COLUMNS = 560
LEAD_COLUMNS = 64
WARM_ROUTING = 5 * 3 * D
WARM_MASKING = 7 * 3 * D
assert slot_of(PASSES[-1]) < C
assert S_GELU[KB - 1] + 2 < slot_of((1, KB - 1, 0, 0))


def build(nc, x, cond, Wx, Wh, Wr, br, W1, b1, W2, b2, out):
    ctx = ExitStack()
    with ctx:
        def sb(name, shape, dt=F32):
            return ctx.enter_context(nc.sbuf_tensor(name, shape, dt))

        def ps(name, shape, dt=F32):
            return ctx.enter_context(nc.psum_tensor(name, shape, dt))

        def sem(name):
            return ctx.enter_context(nc.semaphore(name))

        x_sb = sb("x_sb", [N, NCH, D])
        cond_sb = sb("cond_sb", [B, D])
        Wx_sb = sb("Wx_sb", [D, D])
        Wh_sb = sb("Wh_sb", [D, D])
        Wr_sb = sb("Wr_sb", [D, E])
        br_sb = sb("br_sb", [N, E])
        W1_sb = sb("W1_sb", [D, E, H])
        W2_sb = sb("W2_sb", [128, E, KB, D])
        b_sb = sb("b_sb", [128, H + D])
        Wh_rest = sb("Wh_rest", [D, D])
        Wh_part = sb("Wh_part", [D, 3, D], BF16)
        Wh_16 = sb("Wh_16", [D, D], F16)
        Wr_up = sb("Wr_up", [D, E])
        Wr_rest = sb("Wr_rest", [D, E])
        Wr_part = sb("Wr_part", [D, 3, E], BF16)
        Wr_16 = sb("Wr_16", [D, E], F16)
        br_up = sb("br_up", [N, E])
        W1_rest = sb("W1_rest", [D, E, H])
        W1_part = sb("W1_part", [D, 3, E, H], BF16)
        W1_16 = sb("W1_16", [D, E, H], F16)
        W2_rest = sb("W2_rest", [128, E, KB, D])
        W2_part = sb("W2_part", [128, 3, E, KB, D], BF16)
        W2_16 = sb("W2_16", [128, E, KB, D], F16)
        b_rest = sb("b_rest", [128, H + D])
        b_part = sb("b_part", [128, H + D], BF16)
        ident = sb("ident", [128, 128])
        ident16 = sb("ident16", [128, 128], BF16)
        desc = sb("desc", [N, E])
        x_stage = sb("x_stage", [N, 2, D])
        xT = sb("xT", [D, 2, N])
        h0_up = sb("h0_up", [D, B])
        hi = sb("hi", [D, 2, B, C], F16)
        lo = sb("lo", [D, 2, B, C], F16)
        extreme = sb("extreme", [128, 1 + KB])
        logit = sb("logit", [N, E])
        top = sb("top", [N, 1])
        cand = sb("cand", [N, E])
        first = sb("first", [N, 1])
        onehot = sb("onehot", [128, 4, 32], BF16)
        onehotT = sb("onehotT", [128, N], BF16)
        mask_up = sb("mask_up", [128, E, N], F16)
        mask_one = sb("mask_one", [128, E, N], F16)
        hm_hi = sb("hm_hi", [D, E, N], F16)
        hm_lo = sb("hm_lo", [D, E, N], F16)
        g = sb("g", [128, KB, N])
        g_hi = sb("g_hi", [128, KB, N], F16)
        g_lo = sb("g_lo", [128, KB, N], F16)
        gm_hi = sb("gm_hi", [128, KB, E, N], F16)
        gm_lo = sb("gm_lo", [128, KB, E, N], F16)
        yT = sb("yT", [D, N])
        y_sb = sb("y_sb", [N, 2, D])
        pre = ps("pre", [128, 2, 512])
        state = ps("state", [128, 256, B])
        mask = ps("mask", [128, E, N])
        z = ps("z", [128, 2, 512])
        y = ps("y", [128, 4, 128])
        small = ps("small", [128, 4, 128])

        x0_loaded = sem("x0_loaded")
        x_loaded = sem("x_loaded")
        cond_loaded = sem("cond_loaded")
        wx_loaded = sem("wx_loaded")
        wh_loaded = sem("wh_loaded")
        wr_loaded = sem("wr_loaded")
        w1_loaded = sem("w1_loaded")
        w2_loaded = sem("w2_loaded")
        w2_first_loaded = sem("w2_first_loaded")
        b_loaded = sem("b_loaded")
        ident_zeroed = sem("ident_zeroed")
        ident_ready = sem("ident_ready")
        ident16_ready = sem("ident16_ready")
        desc_ready = sem("desc_ready")
        pads_zeroed = sem("pads_zeroed")
        x_staged = sem("x_staged")
        xT_made = sem("xT_made")
        xT_ready = sem("xT_ready")
        h0_made = sem("h0_made")
        h0_ready = sem("h0_ready")
        wh_split = sem("wh_split")
        wh_16_ready = sem("wh_16_ready")
        wr_split = sem("wr_split")
        b_split = sem("b_split")
        w1_cast = sem("w1_cast")
        w1_rest = sem("w1_rest")
        w2_cast = sem("w2_cast")
        w2_split = sem("w2_split")
        summed = sem("summed")
        h_ready = sem("h_ready")
        lo_ready = sem("lo_ready")
        logits_made = sem("logits_made")
        route_step = sem("route_step")
        onehot_ready = sem("onehot_ready")
        onehotT_made = sem("onehotT_made")
        onehotT_ready = sem("onehotT_ready")
        mask_made = sem("mask_made")
        mask_up_ready = sem("mask_up_ready")
        mask_one_ready = sem("mask_one_ready")
        hm_ready = sem("hm_ready")
        z_made = sem("z_made")
        g_ready = sem("g_ready")
        g_lo_ready = sem("g_lo_ready")
        gm_ready = sem("gm_ready")
        y_made = sem("y_made")
        yT_ready = sem("yT_ready")
        y_turned = sem("y_turned")
        y_ready = sem("y_ready")
        stored = [sem(f"stored_{q}") for q in range(2)]

        block = ctx.enter_context(nc.Block())

        def columns(buf, q, s):
            if buf is pre:
                return pre[:, q, s:s + C + 1:C]
            return buf[:, q, :, s]

        def before(q, s):
            return (q, s - 1) if s else (1 - q, C - 1)

        @block.sync
        def _(sp):
            sp.dma_start(x_sb[:, 0, :], x[:, 0:C, :]).then_inc(x0_loaded, 16)
            sp.dma_start(Wx_sb[:, :], Wx).then_inc(wx_loaded, 16)
            sp.wait_ge(pads_zeroed, 2)
            sp.dma_start(W1_sb[:, :, :], W1.rearrange("e d h -> d e h")).then_inc(w1_loaded, 16)
            for i in range(3):
                sp.dma_start(b_sb[32 * i:32 * i + E, 0:H], b1).then_inc(b_loaded, 16)
                sp.dma_start(b_sb[32 * i:32 * i + E, H:H + D], b2).then_inc(b_loaded, 16)
            for b in range(B):
                sp.dma_start(x_sb[b * C:(b + 1) * C, 1:NCH, :],
                             x[b, C:T, :].rearrange("(c s) d -> s c d", s=C)).then_inc(x_loaded, 16)
            sp.dma_start(W2_sb[:, :, :, :].rearrange("p e k d -> p (e k) d"),
                         W2.rearrange("e (k p) d -> p (e k) d", p=128)).then_inc(w2_loaded, 16)

            def store(c, q):
                sp.wait_ge(y_ready, c + 1)
                sp.dma_start(out[:, bass.ds(c * C, C), :], y_sb[:, q, :]).then_inc(stored[q], 16)

            with sp.Fori(0, NCH // 2) as pair:
                for q in range(2):
                    store(2 * pair + q, q)
            for q in range(2):
                sp.wait_ge(stored[q], 16 * (NCH // 2))

        @block.gpsimd
        def _(pool):
            def stage_x(c, q):
                pool.wait_ge(xT_made, c - 1)
                nc.gpsimd.tensor_copy(x_stage[:, q, :], x_sb[:, c, :]).then_inc(x_staged, 1)

            def split_w2(k):
                w, rest = W2_sb[:, :, k, :], W2_rest[:, :, k, :]
                nc.gpsimd.tensor_tensor(rest, w, W2_part[:, 0, :, k, :], ALU.subtract).then_inc(w2_split, 1)
                pool.wait_ge(w2_split, 3 * k + 1)
                nc.gpsimd.tensor_copy(W2_part[:, 1, :, k, :], rest).then_inc(w2_split, 1)
                pool.wait_ge(w2_split, 3 * k + 2)
                nc.gpsimd.tensor_tensor(W2_part[:, 2, :, k, :], rest, W2_part[:, 1, :, k, :], ALU.subtract)\
                  .then_inc(w2_split, 1)

            pool.dma_start(cond_sb[:, :], cond).then_inc(cond_loaded, 16)
            nc.gpsimd.memset(ident[:, :], 0.0).then_inc(ident_zeroed, 1)
            nc.gpsimd.memset(b_sb[:, :], 0.0).then_inc(pads_zeroed, 1)
            nc.gpsimd.memset(onehot[:, :, :], 0.0).then_inc(pads_zeroed, 1)
            pool.wait_ge(ident_zeroed, 1)
            nc.gpsimd.affine_select(out=ident[:, :], in_=ident[:, :], compare_op=ALU.not_equal, fill=1.0,
                                    base=0, pattern=[[-1, 128]], channel_multiplier=1).then_inc(ident_ready, 1)
            for e in range(E):
                last = nc.gpsimd.memset(desc[:, e:e + 1], float(E - e))
            last.then_inc(desc_ready, 1)
            pool.dma_start(Wr_sb[:, :], Wr).then_inc(wr_loaded, 16)
            pool.dma_start(br_sb[:, :], br.rearrange("(o e) -> o e", o=1).to_broadcast([N, E])).then_inc(wr_loaded, 16)
            pool.dma_start(W2_part[:, 0, :, :, :].rearrange("p e k d -> p (e k) d"),
                           W2.rearrange("e (k p) d -> p (e k) d", p=128)).then_inc(w2_first_loaded, 16)
            pool.wait_ge(wr_loaded, 32)
            nc.gpsimd.tensor_scalar(Wr_up[:, :], Wr_sb[:, :], UP, None, ALU.mult).then_inc(wr_split, 1)
            nc.gpsimd.tensor_scalar(br_up[:, :], br_sb[:, :], UP, None, ALU.mult).then_inc(wr_split, 1)
            nc.gpsimd.tensor_copy(Wr_16[:, :], Wr_sb[:, :]).then_inc(wr_split, 1)
            pool.wait_ge(wr_split, 3)
            nc.gpsimd.tensor_copy(Wr_part[:, 0, :], Wr_up[:, :]).then_inc(wr_split, 1)
            pool.wait_ge(wr_split, 4)
            nc.gpsimd.tensor_tensor(Wr_rest[:, :], Wr_up[:, :], Wr_part[:, 0, :], ALU.subtract).then_inc(wr_split, 1)
            pool.wait_ge(wr_split, 5)
            nc.gpsimd.tensor_copy(Wr_part[:, 1, :], Wr_rest[:, :]).then_inc(wr_split, 1)
            pool.wait_ge(wr_split, 6)
            nc.gpsimd.tensor_tensor(Wr_part[:, 2, :], Wr_rest[:, :], Wr_part[:, 1, :], ALU.subtract)\
              .then_inc(wr_split, 1)
            pool.wait_ge(x_loaded, 16 * B)
            nc.gpsimd.tensor_copy(x_stage[:, 1, :], x_sb[:, 1, :]).then_inc(x_staged, 1)
            pool.wait_ge(w2_loaded, 16)
            pool.wait_ge(w2_first_loaded, 16)
            split_w2(0)
            stage_x(2, 0)
            split_w2(1)
            stage_x(3, 1)
            split_w2(2)
            with pool.Fori(2, NCH // 2) as pair:
                for q in range(2):
                    stage_x(2 * pair + q, q)

        @block.scalar
        def _(act):
            def step(t, q, s):
                act.wait_ge(summed, t + 1)
                nc.scalar.activation(columns(hi, q, s), columns(pre, q, s), ACT.Tanh, scale=1 / UP)
                nc.scalar.activation(state[:, 0, :], columns(pre, q, s), ACT.Tanh, scale=1 / UP).then_inc(h_ready, 1)

            def ffn_slot(c, s):
                if s == S_MASK + 1:
                    act.wait_ge(mask_made, c + 1)
                    nc.scalar.mul(mask_up[:, :, :], mask[:, :, :], UP).then_inc(mask_up_ready, 1)
                for k in range(KB):
                    if s == S_GELU[k]:
                        act.wait_ge(z_made, KB * c + k + 1)
                        nc.scalar.activation(g_hi[:, k, :], z[:, k % 2, 0:N], ACT.Gelu, scale=1 / UP)
                        nc.scalar.activation(g[:, k, :], z[:, k % 2, 0:N], ACT.Gelu, scale=1 / UP)\
                          .then_inc(g_ready, 1)

            def take_y(c):
                act.wait_ge(y_made, c + 1)
                nc.scalar.mul(yT[:, :], y[:, 0, 0:N], 1 / UP).then_inc(yT_ready, 1)

            def cast_w1(e, i):
                if i == 0:
                    nc.scalar.copy(W1_part[:, 0, e, :], W1_sb[:, e, :]).then_inc(w1_cast, 1)
                elif i == 1:
                    nc.scalar.copy(W1_16[:, e, :], W1_sb[:, e, :]).then_inc(w1_cast, 1)
                else:
                    act.wait_ge(w1_rest, 2 * e + 1)
                    nc.scalar.copy(W1_part[:, 1, e, :], W1_rest[:, e, :]).then_inc(w1_cast, 1)

            def cast_w2(k, experts):
                nc.scalar.copy(W2_16[:, experts, k, :], W2_sb[:, experts, k, :]).then_inc(w2_cast, 1)

            act.dma_start(Wh_sb[:, :], Wh).then_inc(wh_loaded, 16)
            act.wait_ge(ident_ready, 1)
            nc.scalar.activation(yT[:, 0:1], ident[:, 0:1], ACT.Gelu)
            act.wait_ge(wh_loaded, 16)
            nc.scalar.copy(Wh_16[:, :], Wh_sb[:, :]).then_inc(wh_16_ready, 1)

            def chunk(c, q, residual=True):
                for s in range(C):
                    step(c * C + s, q, s)
                    if s == 0 and residual:
                        take_y(c - 2)
                    ffn_slot(c - 1, s)

            for s in range(C):
                step(s, 0, s)
                e, i = divmod(s - S_W1, 3)
                if 0 <= e < E:
                    if e == 0 and i == 0:
                        act.wait_ge(w1_loaded, 16)
                    cast_w1(e, i)
            for s in range(C):
                step(C + s, 1, s)
                ffn_slot(0, s)
                k, half = divmod(s - S_HM, 2)
                if 0 <= k < KB:
                    if k == 0 and half == 0:
                        act.wait_ge(w2_loaded, 16)
                    cast_w2(k, slice(half * E // 2, (half + 1) * E // 2))
            with act.Fori(1, NCH // 2) as pair:
                for q in range(2):
                    chunk(2 * pair + q, q)
            for s in range(C):
                if s == 0:
                    take_y(NCH - 2)
                ffn_slot(NCH - 1, s)
            take_y(NCH - 1)

        @block.vector
        def _(dve):
            def low_part(out, v, v_hi, by_product):
                return nc.vector.tensor_tensor_reduce(
                    out=out, in0=v, in1=v_hi, scale=UP, scalar=0.0, op0=ALU.subtract, op1=ALU.max,
                    accum_out=extreme[:, by_product:by_product + 1])

            def split_state(t, q, s):
                dve.wait_ge(h_ready, t + 1)
                low_part(columns(lo, q, s), state[:, 0, :], columns(hi, q, s), 0).then_inc(lo_ready, 1)

            def ffn_slot(c, q, s):
                chunk_hi = hi[:, q:q + 1, :, :].rearrange("p o b s -> p o (b s)").to_broadcast([D, E, N])
                chunk_lo = lo[:, q:q + 1, :, :].rearrange("p o b s -> p o (b s)").to_broadcast([D, E, N])
                if s == 0:
                    dve.wait_ge(logits_made, c + 1)
                    nc.vector.tensor_tensor_reduce(out=logit[:, :], in0=small[0:N, 0, 0:E], in1=br_up[:, :],
                                                   scale=1.0, scalar=-3.0e38, op0=ALU.add, op1=ALU.max,
                                                   accum_out=top[:, :]).then_inc(route_step, 1)
                    dve.wait_ge(route_step, 3 * c + 1)
                    nc.vector.scalar_tensor_tensor(cand[:, :], logit[:, :], top[:, 0:1], desc[:, :],
                                                   ALU.is_equal, ALU.mult).then_inc(route_step, 1)
                    dve.wait_ge(route_step, 3 * c + 2)
                    nc.vector.tensor_reduce(first[:, :], cand[:, :], mybir.AxisListType.X, ALU.max)\
                      .then_inc(route_step, 1)
                elif s == 1:
                    dve.wait_ge(route_step, 3 * c + 3)
                    nc.vector.tensor_scalar(onehot[0:N, 0:3, 0:E],
                                            cand[:, :].rearrange("p (o e) -> p o e", o=1).to_broadcast([N, 3, E]),
                                            first[:, 0:1], None, ALU.is_equal).then_inc(onehot_ready, 1)
                if s == S_HM:
                    dve.wait_ge(mask_up_ready, c + 1)
                    nc.vector.tensor_tensor(hm_hi[:, :, :], mask_up[:, :, :], chunk_hi, ALU.mult).then_inc(hm_ready, 1)
                    nc.vector.tensor_scalar(mask_one[:, :, :], mask_up[:, :, :], 1 / UP, None, ALU.mult)\
                      .then_inc(mask_one_ready, 1)
                elif s == S_HM + 1:
                    dve.wait_ge(mask_one_ready, c + 1)
                    nc.vector.tensor_tensor(hm_lo[:, :, :], mask_one[:, :, :], chunk_lo, ALU.mult).then_inc(hm_ready, 1)
                elif s == S_HM + 2:
                    dve.wait_ge(onehotT_made, c + 1)
                    nc.vector.tensor_scalar(onehotT[:, :], small[:, 1, 0:N], UP, None, ALU.mult)\
                      .then_inc(onehotT_ready, 1)
                for k in range(KB):
                    if s == S_GELU[k]:
                        dve.wait_ge(g_ready, KB * c + k + 1)
                        low_part(g_lo[:, k, :], g[:, k, :], g_hi[:, k, :], 1 + k).then_inc(g_lo_ready, 1)
                    elif s == S_GELU[k] + 1:
                        nc.vector.tensor_tensor(gm_hi[:, k, :, :], mask_up[:, :, :],
                                                g_hi[:, k:k + 1, :].to_broadcast([128, E, N]), ALU.mult)\
                          .then_inc(gm_ready, 1)
                    elif s == S_GELU[k] + 2:
                        dve.wait_ge(g_lo_ready, KB * c + k + 1)
                        nc.vector.tensor_tensor(gm_lo[:, k, :, :], mask_one[:, :, :],
                                                g_lo[:, k:k + 1, :].to_broadcast([128, E, N]), ALU.mult)\
                          .then_inc(gm_ready, 1)

            def add_residual(c, q):
                dve.wait_ge(y_turned, c + 1)
                dve.wait_ge(stored[q], 8 * (c - q))
                nc.vector.tensor_tensor(y_sb[:, q, :], y[0:N, 1, :], x_sb[:, c, :], ALU.add).then_inc(y_ready, 1)

            def take_xT(c, q):
                dve.wait_ge(xT_made, c + 1)
                nc.vector.tensor_scalar(xT[:, q, :], y[:, 2, 0:N], UP, None, ALU.mult).then_inc(xT_ready, 1)

            def split_w1(e, i):
                if i == 1:
                    dve.wait_ge(w1_cast, 3 * e + 1)
                    nc.vector.tensor_tensor(W1_rest[:, e, :], W1_sb[:, e, :], W1_part[:, 0, e, :], ALU.subtract)\
                      .then_inc(w1_rest, 1)
                elif i == 3:
                    dve.wait_ge(w1_cast, 3 * e + 3)
                    nc.vector.tensor_tensor(W1_part[:, 2, e, :], W1_rest[:, e, :], W1_part[:, 1, e, :], ALU.subtract)\
                      .then_inc(w1_rest, 1)

            dve.wait_ge(ident_ready, 1)
            nc.vector.tensor_copy(ident16[:, :], ident[:, :]).then_inc(ident16_ready, 1)
            take_xT(0, 0)
            dve.wait_ge(h0_made, 1)
            nc.vector.tensor_scalar(h0_up[:, :], y[:, 3, 0:B], UP, None, ALU.mult).then_inc(h0_ready, 1)

            def split(w, rest, part, done, count):
                nc.vector.tensor_scalar(part[0], w, UP, None, ALU.mult).then_inc(done, 1)
                dve.wait_ge(done, count + 1)
                nc.vector.scalar_tensor_tensor(rest, w, UP, part[0], ALU.mult, ALU.subtract).then_inc(done, 1)
                dve.wait_ge(done, count + 2)
                nc.vector.tensor_copy(part[1], rest).then_inc(done, 1)
                dve.wait_ge(done, count + 3)
                nc.vector.tensor_tensor(part[2], rest, part[1], ALU.subtract).then_inc(done, 1)

            dve.wait_ge(pads_zeroed, 2)
            dve.wait_ge(desc_ready, 1)
            dve.wait_ge(wh_loaded, 16)
            split(Wh_sb[:, :], Wh_rest[:, :], [Wh_part[:, i, :] for i in range(3)], wh_split, 0)

            def first_chunk_slot(s):
                if s == B_STEPS[0]:
                    dve.wait_ge(b_loaded, 16 * 6)
                    nc.vector.tensor_copy(b_part[:, :], b_sb[:, :]).then_inc(b_split, 1)
                elif s == B_STEPS[1]:
                    dve.wait_ge(b_split, 1)
                    nc.vector.tensor_tensor(b_rest[:, 0:H], b_sb[:, 0:H], b_part[:, 0:H], ALU.subtract)\
                      .then_inc(b_split, 1)
                elif s == B_STEPS[2]:
                    nc.vector.tensor_tensor(b_rest[:, H:H + D], b_sb[:, H:H + D], b_part[:, H:H + D],
                                            ALU.subtract).then_inc(b_split, 1)
                elif s in B_STEPS[3:5]:
                    i = B_STEPS.index(s) - 2
                    dve.wait_ge(b_split, 3)
                    nc.vector.tensor_copy(b_part[32 * i:32 * i + 32, :], b_rest[32 * i:32 * i + 32, :])\
                      .then_inc(b_split, 1)
                elif s == B_STEPS[5]:
                    dve.wait_ge(b_split, 5)
                    nc.vector.tensor_tensor(b_part[64:96, :], b_rest[64:96, :], b_part[64:96, :], ALU.subtract)\
                      .then_inc(b_split, 1)

            def chunk(c, q, residual=True, ahead=True):
                for s in range(C):
                    split_state(c * C + s, q, s)
                    ffn_slot(c - 1, 1 - q, s)
                    if s == S_STORE and residual:
                        add_residual(c - 2, q)
                    if s == S_XT and ahead:
                        take_xT(c + 1, 1 - q)

            for s in range(C):
                split_state(s, 0, s)
                for e in range(E):
                    split_w1(e, s - S_W1 - 3 * e)
                first_chunk_slot(s)
                if s == S_XT0 + 1:
                    take_xT(1, 1)
            chunk(1, 1, residual=False)
            for c in range(2, NCH):
                chunk(c, c % 2, ahead=c + 1 < NCH)
            for s in range(C):
                ffn_slot(NCH - 1, 1, s)
                if s == S_STORE:
                    add_residual(NCH - 2, 0)
            add_residual(NCH - 1, 1)

        @block.tensor
        def _(pe):
            def keep_warm(q, count, start=False):
                stream = Wh_part[:, :, :].rearrange("p i d -> p (i d)")
                while count > 0:
                    n = min(count, 3 * D)
                    nc.tensor.matmul(pre[:, q, N:N + n], Wh_16[:, :], stream[:, 0:n], start=start, stop=True,
                                     skip_group_check=True)
                    count -= n

            def transpose_x(c, q, start=False):
                pe.wait_ge(x_staged, c)
                keep_warm(q, LEAD_COLUMNS, start)
                nc.tensor.transpose(y[:, 2, 0:N], x_stage[:, q, :], ident[0:N, 0:N]).then_inc(xT_made, 1)

            def project_x(c, q, half):
                if half == 0:
                    pe.wait_ge(xT_ready, c + 1)
                own = slice(half * D // 2, (half + 1) * D // 2)
                nc.tensor.matmul(pre[own, q, 0:N], Wx_sb[:, own], xT[:, q, :], start=True, stop=True)

            def step(t, q, s):
                def add_state(part, state_part):
                    return nc.tensor.matmul(columns(pre, q, s), part, state_part, start=False, stop=True,
                                            skip_group_check=True)

                pe.wait_ge(h_ready, t)
                for i in (2, 1, 0):
                    add_state(Wh_part[:, i, :], columns(hi, *before(q, s)))
                keep_warm(q, GAP_COLUMNS)
                pe.wait_ge(lo_ready, t)
                add_state(Wh_16[:, :], columns(lo, *before(q, s))).then_inc(summed, 1)

            def ffn_pass(c, layer, k, e, part):
                if (e, part) == BIAS:
                    if layer == 0:
                        if k == 0:
                            pe.wait_ge(onehotT_ready, c + 1)
                        nc.tensor.matmul(z[:, k % 2, 0:N], b_part[:, k * 128:(k + 1) * 128], onehotT[:, :],
                                         start=False, stop=True).then_inc(z_made, 1)
                    else:
                        nc.tensor.matmul(y[:, 0, 0:N], b_part[:, H:H + D], onehotT[:, :], start=False, stop=True)\
                          .then_inc(y_made, 1)
                elif layer == 0:
                    if e == 0 and part == 0 and k == 0:
                        pe.wait_ge(hm_ready, 2 * c + 1)
                    elif e == 0 and part == 3 and k == 0:
                        pe.wait_ge(hm_ready, 2 * c + 2)
                    elif e == 0 and part == 0 and k >= 2:
                        pe.wait_ge(g_ready, KB * c + k - 1)
                    cols = slice(k * 128, (k + 1) * 128)
                    if part < 3:
                        nc.tensor.matmul(z[:, k % 2, 0:N], W1_part[:, part, e, cols], hm_hi[:, e, :],
                                         start=(e == 0 and part == 0), stop=False)
                    else:
                        nc.tensor.matmul(z[:, k % 2, 0:N], W1_16[:, e, cols], hm_lo[:, e, :], start=False, stop=False)
                else:
                    if e == 0 and part == 0:
                        pe.wait_ge(gm_ready, 2 * (KB * c + k) + 1)
                    elif e == 0 and part == 3:
                        pe.wait_ge(gm_ready, 2 * (KB * c + k) + 2)
                    if part < 3:
                        nc.tensor.matmul(y[:, 0, 0:N], W2_part[:, part, e, k, :], gm_hi[:, k, e, :],
                                         start=(k == 0 and e == 0 and part == 0), stop=False)
                    else:
                        nc.tensor.matmul(y[:, 0, 0:N], W2_16[:, e, k, :], gm_lo[:, k, e, :], start=False, stop=False)

            def turn_y(c, q):
                pe.wait_ge(yT_ready, c + 1)
                keep_warm(1 - q, LEAD_COLUMNS)
                nc.tensor.transpose(y[0:N, 1, :], yT[:, :], ident[:, :]).then_inc(y_turned, 1)

            def ffn_slot(c, q, s, first=False):
                if s == 0:
                    chunk_hi = hi[:, q, :, :].rearrange("p b s -> p (b s)")
                    chunk_lo = lo[:, q, :, :].rearrange("p b s -> p (b s)")
                    for i in range(3):
                        nc.tensor.matmul(small[0:N, 0, 0:E], chunk_hi, Wr_part[:, i, :], start=(i == 0), stop=False)
                    nc.tensor.matmul(small[0:N, 0, 0:E], chunk_lo, Wr_16[:, :], start=False, stop=True)\
                      .then_inc(logits_made, 1)
                if s == S_MASK:
                    pe.wait_ge(onehot_ready, c + 1)
                    for e in range(E):
                        last = nc.tensor.matmul(mask[:, e, :], onehot[:, 0, e:e + 1].to_broadcast([128, 128]),
                                                ident16[:, 0:N], start=True, stop=True)
                    last.then_inc(mask_made, 1)
                elif s == S_MASK + 1:
                    nc.tensor.matmul(small[:, 1, 0:N], onehot[:, :, :].rearrange("p i e -> p (i e)"),
                                     ident16[:, 0:N], start=True, stop=True).then_inc(onehotT_made, 1)
                for layer, k, e, part in passes_behind(s):
                    if first and (layer, k, e, part) == PASSES[0]:
                        pe.wait_ge(w1_cast, 3 * E)
                        pe.wait_ge(w1_rest, 2 * E)
                        pe.wait_ge(b_split, 6)
                    if first and layer == 1 and (e, part) == (0, 0):
                        pe.wait_ge(w2_cast, 2 * (k + 1))
                        pe.wait_ge(w2_split, 3 * (k + 1))
                    ffn_pass(c, layer, k, e, part)

            pe.wait_ge(ident_ready, 1)
            pe.wait_ge(x0_loaded, 16)
            nc.tensor.transpose(y[:, 2, 0:N], x_sb[:, 0, :], ident[0:N, 0:N]).then_inc(xT_made, 1)
            pe.wait_ge(cond_loaded, 16)
            pe.wait_ge(xT_ready, 1)
            nc.tensor.transpose(y[:, 3, 0:B], cond_sb[:, :], ident[0:B, 0:B]).then_inc(h0_made, 1)
            pe.wait_ge(wx_loaded, 16)
            project_x(0, 0, 0)
            project_x(0, 0, 1)
            pe.wait_ge(wh_loaded, 16)
            pe.wait_ge(h0_ready, 1)
            nc.tensor.matmul(columns(pre, 0, 0), Wh_sb[:, :], h0_up[:, :], start=False, stop=True,
                             skip_group_check=True).then_inc(summed, 1)
            pe.wait_ge(wh_split, 4)
            pe.wait_ge(wh_16_ready, 1)

            def chunk(c, q, first=False, residual=True, ahead=True):
                for s in range(C):
                    step(c * C + s, q, s)
                    ffn_slot(c - 1, 1 - q, s, first)
                    if s == S_TURN and residual:
                        turn_y(c - 2, q)
                    if ahead:
                        if s == S_XT:
                            if residual:
                                pe.wait_ge(y_ready, c - 1)
                            transpose_x(c + 1, 1 - q)
                        elif s in S_XP:
                            project_x(c + 1, 1 - q, S_XP.index(s))
                    keep_warm(1 - q, SLOT_COLUMNS - columns_behind(s))

            for s in range(C):
                if s:
                    step(s, 0, s)
                if s == S_XT0:
                    transpose_x(1, 1, start=True)
                elif s in S_XP0:
                    project_x(1, 1, S_XP0.index(s))
                elif s == C - 1:
                    pe.wait_ge(wr_split, 7)
                if s:
                    keep_warm(1, SLOT_COLUMNS, start=s < S_XP0[0])
            chunk(1, 1, first=True, residual=False)
            with pe.Fori(1, NCH // 2 - 1) as pair:
                for q in range(2):
                    chunk(2 * pair + q, q)
            chunk(NCH - 2, 0)
            chunk(NCH - 1, 1, ahead=False)
            pe.wait_ge(lo_ready, T)
            for s in range(C):
                if s == S_MASK:
                    keep_warm(0, WARM_ROUTING)
                elif s == S_MM:
                    keep_warm(0, WARM_MASKING)
                ffn_slot(NCH - 1, 1, s)
                if s == S_TURN:
                    turn_y(NCH - 2, 0)
            turn_y(NCH - 1, 1)


_INS = ["x", "cond_1024", "L0_cond_Wx", "L0_cond_Wh", "L0_ffn_Wr", "L0_ffn_br", "L0_ffn_W1", "L0_ffn_b1",
        "L0_ffn_W2", "L0_ffn_b2"]
_OUTS = [((B, T, D), "float32")]


def kernel(**inputs):
    import numpy as _np
    import concourse.bacc as _bacc
    from concourse import mybir as _mybir
    from concourse.bass_utils import run_bass_kernel_spmd as _run

    nc = _bacc.Bacc("TRN2", target_bir_lowering=False, num_devices=1)
    arrays, args = {}, []
    for name in _INS:
        a = _np.ascontiguousarray(inputs[name])
        arrays[f"in_{name}_dram"] = a
        args.append(nc.dram_tensor(f"in_{name}_dram", a.shape, _mybir.dt.from_np(a.dtype), kind="ExternalInput").ap())
    for i, (shape, dtype) in enumerate(_OUTS):
        dt = _mybir.dt.from_np(_np.dtype(dtype))
        args.append(nc.dram_tensor(f"out_{i}_dram", shape, dt, kind="ExternalOutput").ap())
    build(nc, *args)
    r = _run(nc, [arrays], core_ids=[0])
    got = tuple(r.results[0][f"out_{i}_dram"] for i in range(len(_OUTS)))
    return got[0]
```
